# Optimizing a Trainium2 kernel written in Bass

```python
import numpy as np
import jax
import jax.numpy as jnp

def _softmax(x, axis=-1):
    return jax.nn.softmax(x, axis=axis)

def _gelu(x):
    return jax.nn.gelu(x, approximate=True)

def _silu(x):
    return jax.nn.silu(x)

def _sigmoid(x):
    return jax.nn.sigmoid(x)

def _layernorm(x, axis=-1, eps=1e-05):
    m = jnp.mean(x, axis=axis, keepdims=True)
    v = jnp.var(x, axis=axis, keepdims=True)
    return (x - m) / jnp.sqrt(v + eps)

def _scatter_add(tgt, idx, src, axis=0):
    return tgt.at[idx].add(src)

def _segment_sum(src, seg, n):
    return jax.ops.segment_sum(src, seg, n)
kernel_name = 'mk_prb_d1_jaxref_r4_0c5936'

def setup_inputs(seed: int=0):
    np.random.seed(seed)
    _w = jnp.asarray

    def _L0_attn_setup():
        import jax, jax.numpy as jnp
        import numpy as np
        HIDDEN = 512
        KEY = 512
        EPS = 1e-05
        key = jax.random.key(seed)
        k1, k2, k3 = jax.random.split(key, 3)
        B, S = (4, 512)
        x = jax.random.normal(k1, (B, S, HIDDEN), dtype=jnp.float32)
        bq = 1.0 / np.sqrt(HIDDEN)
        qkv = jax.random.uniform(k2, (HIDDEN, KEY * 3), minval=-bq, maxval=bq, dtype=jnp.float32)
        bo = 1.0 / np.sqrt(KEY)
        o_proj = jax.random.uniform(k3, (KEY, HIDDEN), minval=-bo, maxval=bo, dtype=jnp.float32)
        gamma = jnp.ones((HIDDEN,), dtype=jnp.float32)
        beta = jnp.zeros((HIDDEN,), dtype=jnp.float32)
        return {'x': x, 'qkv': qkv, 'o_proj': o_proj, 'gamma': gamma, 'beta': beta}
    _L0_attn_in = _L0_attn_setup()

    def _L0_ffn_setup():
        import jax, jax.numpy as jnp
        import numpy as np

        def _sparsify_2to4(h):
            B, S, I = h.shape
            g = h.reshape(B, S, I // 4, 4)
            a = jnp.abs(g)
            _, idx = jax.lax.top_k(a, 2)
            pos = jnp.arange(4)
            mask = (pos == idx[..., 0:1]) | (pos == idx[..., 1:2])
            return (g * mask.astype(g.dtype)).reshape(B, S, I)
        key = jax.random.key(seed)
        k1, k2, k3, k4 = jax.random.split(key, 4)
        B, S, H, I = (4, 512, 512, 2048)
        x = jax.random.normal(k1, (B, S, H), dtype=jnp.float32)
        w_gate = jax.random.normal(k2, (H, I), dtype=jnp.float32) / np.sqrt(H)
        w_up = jax.random.normal(k3, (H, I), dtype=jnp.float32) / np.sqrt(H)
        w_down = jax.random.normal(k4, (I, H), dtype=jnp.float32) / np.sqrt(I)
        return {'x': x, 'w_gate': w_gate, 'w_up': w_up, 'w_down': w_down}
    _L0_ffn_in = _L0_ffn_setup()
    _d = {'L0_attn_x': _L0_attn_in['x'], 'L0_attn_qkv': _L0_attn_in['qkv'], 'L0_attn_o_proj': _L0_attn_in['o_proj'], 'L0_attn_gamma': _L0_attn_in['gamma'], 'L0_attn_beta': _L0_attn_in['beta'], 'L0_ffn_w_gate': _L0_ffn_in['w_gate'], 'L0_ffn_w_up': _L0_ffn_in['w_up'], 'L0_ffn_w_down': _L0_ffn_in['w_down']}
    _x0 = _d['L0_attn_x']
    _d['L0_attn_x'] = jax.random.normal(jax.random.fold_in(jax.random.key(seed), 1), (1, 2048, 512), dtype=_x0.dtype)
    del _x0
    return _d

def reference(L0_attn_x, L0_attn_qkv, L0_attn_o_proj, L0_attn_gamma, L0_attn_beta, L0_ffn_w_gate, L0_ffn_w_up, L0_ffn_w_down):

    def _L0_attn_ref(x, qkv, o_proj, gamma, beta):
        import jax, jax.numpy as jnp
        import numpy as np
        HIDDEN = 512
        KEY = 512
        EPS = 1e-05
        residual = x
        mu = jnp.mean(x, axis=-1, keepdims=True)
        var = jnp.mean((x - mu) ** 2, axis=-1, keepdims=True)
        x_norm = (x - mu) / jnp.sqrt(var + EPS) * gamma + beta
        q = x_norm @ qkv[:, :KEY]
        k = x_norm @ qkv[:, KEY:2 * KEY]
        v = x_norm @ qkv[:, 2 * KEY:]
        scale = 1.0 / jnp.sqrt(jnp.float32(KEY))
        scores = jnp.einsum('bsk,btk->bst', q, k) * scale
        S_len = x.shape[1]
        causal = jnp.tril(jnp.ones((S_len, S_len), dtype=bool))
        scores = jnp.where(causal[None], scores, -jnp.inf)
        attn = jax.nn.softmax(scores, axis=-1)
        out = attn @ v
        out = out @ o_proj
        return out + residual

    def _L0_ffn_ref(x, w_gate, w_up, w_down):
        import jax, jax.numpy as jnp
        import numpy as np

        def _sparsify_2to4(h):
            B, S, I = h.shape
            g = h.reshape(B, S, I // 4, 4)
            a = jnp.abs(g)
            _, idx = jax.lax.top_k(a, 2)
            pos = jnp.arange(4)
            mask = (pos == idx[..., 0:1]) | (pos == idx[..., 1:2])
            return (g * mask.astype(g.dtype)).reshape(B, S, I)
        h = jax.nn.silu(jnp.einsum('bsh,hi->bsi', x, w_gate)) * jnp.einsum('bsh,hi->bsi', x, w_up)
        h_sparse = _sparsify_2to4(h)
        return jnp.einsum('bsi,ih->bsh', h_sparse, w_down)
    x = L0_attn_x
    xn = _layernorm(x, axis=-1)
    x = x + _L0_attn_ref(xn, L0_attn_qkv, L0_attn_o_proj, L0_attn_gamma, L0_attn_beta) + _L0_ffn_ref(xn, L0_ffn_w_gate, L0_ffn_w_up, L0_ffn_w_down)
    return x

_drawn_inputs = setup_inputs


def setup_inputs(seed=0):
    import zlib

    import numpy as np

    out = dict(_drawn_inputs(seed))
    spreads = {'L0_attn_gamma': (1.0, 0.6), 'L0_attn_beta': (0.0, 0.526)}
    factors = {'L0_attn_qkv': 3.124, 'L0_attn_o_proj': 2.993}
    for name, (base, spread) in spreads.items():
        noise = np.random.default_rng([zlib.crc32(name.encode()), seed]).standard_normal(out[name].shape)
        drawn = base * np.exp(spread * noise) if base else spread * noise
        out[name] = jnp.asarray(drawn.astype(out[name].dtype))
    for name, factor in factors.items():
        out[name] = (out[name] * factor).astype(out[name].dtype)
    return out
```

```python
from contextlib import ExitStack

import concourse.bass as bass
from concourse import mybir

ALU = mybir.AluOpType
ACT = mybir.ActivationFunctionType
AX = mybir.AxisListType
F32 = mybir.dt.float32
F32R = mybir.dt.float32r
BF16 = mybir.dt.bfloat16

P = 128
W = 512
EPS = 1e-5
MASKED = -3.0e38


def attention_ffn(nc, x, qkv, o_proj, gamma, beta, w_gate, w_up, w_down, out):
    _, S, D = x.shape
    I = w_gate.shape[1]
    KT = D // P
    NT = S // P
    NCH = S // W
    TC = W // P
    G = 4
    NJ = I // (G * P)
    SCALE = float(D) ** -0.5
    assert D == W and KT == TC == G and NJ >= 2

    x_chunks = x.rearrange("a (c t p) d -> (a c) p t d", t=TC, p=P)
    x_tiles = x.rearrange("a (n p) d -> (a n) p d", p=P)
    out_tiles = out.rearrange("a (n p) d -> (a n) p d", p=P)
    out_chunks = out.rearrange("a (c t p) d -> (a c) p t d", t=TC, p=P)
    qkv_k = qkv.rearrange("(k p) n -> p k n", p=P)
    o_proj_k = o_proj.rearrange("(k p) n -> p k n", p=P)
    gate_k = w_gate.rearrange("(k p) i -> p k i", p=P)
    up_k = w_up.rearrange("(k p) i -> p k i", p=P)
    down_j = w_down.rearrange("(j p r) d -> j p r d", p=P, r=G)
    xnT_hi_dram = nc.dram_tensor("xnT_hi", (NCH, KT, P, W), F32, kind="Internal").ap()
    xnT_lo_dram = nc.dram_tensor("xnT_lo", (NCH, KT, P, W), F32, kind="Internal").ap()
    resid_dram = nc.dram_tensor("resid", (NT, P, D), F32, kind="Internal").ap()

    steps = [("x_norm", 0), ("w_turn", 0), ("w_turn", 1), ("x_affine", 0), ("qk_weight", 0), ("w_turn", 2),
             ("x_norm", 1), ("vo_weight", 0), ("x_affine", 1), ("z", 0), ("v", 0), ("scores", 0)]
    for i in range(NT):
        c = i // TC + 1
        if i % TC == TC - 1 and c < NCH:
            steps += [("z", c), ("v", c)]
        if i + 1 < NT:
            steps.append(("scores", i + 1))
        steps.append(("attend", i))
        if i % TC == 0 and c + 1 < NCH:
            steps.append(("x_norm", c + 1))
        if i % TC == 1 and c + 1 < NCH:
            steps.append(("x_affine", c + 1))

    def key_tiles(i):
        return [range(g, min(g + TC, i + 1)) for g in range(0, i + 1, TC)]

    turn_no, prod_no, split_no, group_no = {}, {}, {}, {}
    turned_hi_no = {}
    for kind, n in steps:
        if kind in ("x_norm", "x_affine", "w_turn"):
            for k in range(KT):
                turn_no[kind, n, k] = len(turn_no)
                turned_hi_no[kind, n, k] = len(turned_hi_no)
        elif kind == "attend":
            for g in range(len(key_tiles(n))):
                turn_no[kind, n, g] = len(turn_no)
                turned_hi_no[kind, n, g] = len(turned_hi_no)
                group_no[n, g] = len(group_no)
        elif kind == "scores":
            for g in range(len(key_tiles(n))):
                prod_no[kind, n, g] = len(prod_no)
        else:
            for k in range(KT):
                prod_no[kind, n, k] = len(prod_no)
                split_no[kind, n, k] = len(split_no)
    PROD_RING, TURN_RING, OUT_RING, PT_RING = 4, 2, 2, 2

    with ExitStack() as ctx:
        def sem(name):
            return ctx.enter_context(nc.semaphore(name))

        def sb(name, shape, dt, where=ctx):
            return where.enter_context(nc.sbuf_tensor(name, shape, dt))

        bank = [ctx.enter_context(nc.psum_tensor(f"bank{b}", [P, W], F32)) for b in range(8)]
        prod_bank, turn_bank, o_bank = bank[0:4], bank[4:6], bank[6:8]
        gate_bank, up_bank, down_bank = bank[0:2], bank[2:4], bank[4:8]

        xT_hi, xT_lo = sb("xT_hi", [P, KT, S], F32R), sb("xT_lo", [P, KT, S], F32R)
        zg_hi, zg_lo = sb("zg_hi", [P, KT, W], F32R), sb("zg_lo", [P, KT, W], F32R)
        mu_hi, mu_lo = sb("mu_hi", [P, KT, W], F32R), sb("mu_lo", [P, KT, W], F32R)
        raw = sb("raw", [P, 2, G * W], F32)
        rows = sb("rows", [P, 2, W], F32)
        ident = sb("ident", [P, P], F32)
        causal = sb("causal", [P, P], F32)
        gamma_t, beta_t = sb("gamma_t", [P, KT], F32), sb("beta_t", [P, KT], F32)
        neg_half = sb("neg_half", [P, TC], F32)
        stats = sb("stats", [P, TC, 6], F32)
        mean_var = sb("mean_var", [P, TC, 2], F32)
        var_eps, rstd = sb("var_eps", [P, TC], F32), sb("rstd", [P, TC], F32)
        one_rstd, neg_mean_rstd = sb("one_rstd", [P, NT], F32), sb("neg_mean_rstd", [P, NT], F32)
        part_max = sb("part_max", [P, 2, NCH + 1], F32)
        row_max, neg_max = sb("row_max", [P, 2], F32), sb("neg_max", [P, 2], F32)
        row_sum, inv_sum = sb("row_sum", [P, NT], F32), sb("inv_sum", [P, NT], F32)

        with ExitStack() as early:
            sb("pad_hi", [P, 2 * TC, W], F32, early)
            wv_raw = sb("wv_raw", [P, KT, W], F32, early)
            xw = sb("xw", [P, TC, D], F32, early)
            sb("pad_lo", [P, 2 * TC, W], F32, early)
            wo_raw = sb("wo_raw", [P, KT, W], F32, early)
            stage_hi, stage_lo = sb("stage_hi", [P, 2, W], F32R, early), sb("stage_lo", [P, 2, W], F32R, early)
        with ExitStack() as attention:
            v_hi, v_lo = sb("v_hi", [P, NT, D], F32R, attention), sb("v_lo", [P, NT, D], F32R, attention)
            pT_hi, pT_lo = sb("pT_hi", [P, PT_RING, W], F32R, attention), sb("pT_lo", [P, PT_RING, W], F32R, attention)
            vo_hi, vo_lo = sb("vo_hi", [P, KT, W], F32R, attention), sb("vo_lo", [P, KT, W], F32R, attention)
        with ExitStack() as ffn:
            acc = sb("acc", [P, NT, D], F32, ffn)
            dw_hi, dw_lo = sb("dw_hi", [P, G, D], F32R, ffn), sb("dw_lo", [P, G, D], F32R, ffn)
            hs_hi, hs_lo = sb("hs_hi", [P, G, W], F32R, ffn), sb("hs_lo", [P, G, W], F32R, ffn)
            hid = sb("hid", [P, G, W], F32, ffn)
            mag = sb("mag", [P, G, W], F32, ffn)
            beats_a, beats_b = sb("beats_a", [P, 2, W], BF16, ffn), sb("beats_b", [P, 2, W], BF16, ffn)
            beats_c, pair_sum = sb("beats_c", [P, 2, W], BF16, ffn), sb("pair_sum", [P, 2, W], BF16, ffn)
        turned = [(xT_hi[:, :, 2 * W:3 * W], xT_lo[:, :, 2 * W:3 * W]), (xT_hi[:, :, 3 * W:4 * W], xT_lo[:, :, 3 * W:4 * W]),
                  (v_hi[:, TC:2 * TC, :], v_lo[:, TC:2 * TC, :])]
        wo_hi, wo_lo = v_hi[:, 0:TC, :], v_lo[:, 0:TC, :]
        w_raw = [raw[:, 0, :].rearrange("p (k n) -> p k n", k=KT), raw[:, 1, :].rearrange("p (k n) -> p k n", k=KT), wv_raw[:]]

        x_loaded, affine_loaded, wo_loaded = sem("x_loaded"), sem("affine_loaded"), sem("wo_loaded")
        w_loaded = [sem("wq_loaded"), sem("wk_loaded"), sem("wv_loaded")]
        resid_stored = sem("resid_stored")
        xnT_stored = [sem("xnT_stored0"), sem("xnT_stored1")]
        rows_loaded = [sem("rows_loaded0"), sem("rows_loaded1")]
        consts_ready, pool_step = sem("consts_ready"), sem("pool_step")
        stats_ready, rstd_ready, x_ready = sem("stats_ready"), sem("rstd_ready"), sem("x_ready")
        turn_full, turn_affine, turn_hi, turn_free = sem("turn_full"), sem("turn_affine"), sem("turn_hi"), sem("turn_free")
        prod_full, prod_hi, prod_free = sem("prod_full"), sem("prod_hi"), sem("prod_free")
        wo_hi_ready, wo_ready = sem("wo_hi_ready"), sem("wo_ready")
        vec_step = sem("vec_step")
        max_ready, exp_ready, group_attended, rows_ready = sem("max_ready"), sem("exp_ready"), sem("group_attended"), sem("rows_ready")
        raw_loaded = {m: sem(f"{m}_raw_loaded") for m in ("gate", "up", "down")}
        wt_hi = {m: sem(f"{m}_hi_ready") for m in ("gate", "up", "down")}
        wt_lo = {m: sem(f"{m}_lo_ready") for m in ("gate", "up", "down")}
        xnT_loaded = [sem(f"xnT_loaded{c}") for c in range(NCH)]
        acc_loaded = sem("acc_loaded")
        gate_full, up_full, silu_ready, hid_ready, mag_ready = (sem(n) for n in ("gate_full", "up_full", "silu_ready", "hid_ready", "mag_ready"))
        pick_step, picked, hs_hi_ready, hs_ready = (sem(n) for n in ("pick_step", "picked", "hs_hi_ready", "hs_ready"))
        down_full, added, out_stored = sem("down_full"), sem("added"), sem("out_stored")
        PICK = 11

        block = ctx.enter_context(nc.Block())

        def raw_slot(m):
            return raw[:, 1 if m == "up" else 0, :].rearrange("p (k n) -> p k n", k=G)

        def split_view(m):
            return raw_slot(m).rearrange("p k (g r) -> p k g r", r=G) if m != "down" else raw_slot(m)

        weight_hi = {"gate": zg_hi, "up": mu_hi, "down": dw_hi}
        weight_lo = {"gate": zg_lo, "up": mu_lo, "down": dw_lo}

        def piece(m, r, t):
            return t[:, :, r * P:(r + 1) * P] if m != "down" else t[:, r, :]

        def raw_piece(m, r):
            return split_view(m)[:, :, :, r] if m != "down" else raw_slot(m)[:, r, :]

        last_turn = {i: turn_no["attend", i, len(key_tiles(i)) - 1] + 1 for i in range(NT)}

        @block.sync
        def _(sp):
            def load_x(c):
                if c >= 1:
                    sp.wait_ge(turn_full, turn_no["x_affine", c - 1, KT - 1] + 1)
                sp.dma_start(xw[:], x_chunks[c]).then_inc(x_loaded, 16)

            load_x(0)
            for m in range(2):
                sp.dma_start(w_raw[m], qkv_k[:, :, m * D:(m + 1) * D]).then_inc(w_loaded[m], 16)
            sp.dma_start(gamma_t[:], gamma).then_inc(affine_loaded, 16)
            sp.dma_start(beta_t[:], beta).then_inc(affine_loaded, 16)
            sp.dma_start(w_raw[2], qkv_k[:, :, 2 * D:3 * D]).then_inc(w_loaded[2], 16)
            sp.dma_start(wo_raw[:], o_proj_k).then_inc(wo_loaded, 16)
            for kind, n in steps:
                if kind == "x_norm":
                    for k in range(KT):
                        sp.wait_ge(turn_free, turn_no[kind, n, k] + 1)
                        sp.dma_start(xnT_hi_dram[n, k], stage_hi[:, k % 2, :].bitcast(F32)).then_inc(xnT_stored[k % 2], 16)
                        sp.dma_start(xnT_lo_dram[n, k], stage_lo[:, k % 2, :].bitcast(F32)).then_inc(xnT_stored[k % 2], 16)
                elif kind == "x_affine" and n + 1 < NCH:
                    load_x(n + 1)
                elif kind == "scores":
                    if n >= 2:
                        sp.wait_ge(rows_ready, n - 1)
                        sp.dma_start(resid_dram[n - 2], rows[:, n % 2, :]).then_inc(resid_stored, 16)
                        sp.wait_ge(resid_stored, 16 * (n - 1))
                    sp.dma_start(rows[:, n % 2, :], x_tiles[n]).then_inc(rows_loaded[n % 2], 16)
            sp.wait_ge(turn_full, last_turn[NT - 2])
            sp.dma_start(raw_slot("gate"), gate_k[:, :, 0:G * P]).then_inc(raw_loaded["gate"], 16)
            sp.wait_ge(prod_full, len(prod_no))
            for stored in xnT_stored:
                sp.wait_ge(stored, 16 * KT * NCH)
            for c in range(NCH):
                cols = slice(c * W, (c + 1) * W)
                sp.dma_start(xT_hi[:, :, cols].bitcast(F32), xnT_hi_dram[c].rearrange("k p s -> p k s")).then_inc(xnT_loaded[c], 16)
                sp.dma_start(xT_lo[:, :, cols].bitcast(F32), xnT_lo_dram[c].rearrange("k p s -> p k s")).then_inc(xnT_loaded[c], 16)
                if c == 0:
                    sp.wait_ge(turn_full, last_turn[NT - 1])
                    sp.dma_start(raw_slot("up"), up_k[:, :, 0:G * P]).then_inc(raw_loaded["up"], 16)
            for i in (NT - 2, NT - 1):
                sp.wait_ge(rows_ready, i + 1)
                sp.dma_start(resid_dram[i], rows[:, i % 2, :]).then_inc(resid_stored, 16)
            sp.wait_ge(resid_stored, 16 * NT)
            for c in range(NCH):
                sp.dma_start(acc[:, TC * c:TC * (c + 1), :],
                             resid_dram[TC * c:TC * (c + 1)].rearrange("t p d -> p t d")).then_inc(acc_loaded, 16)

            def down_weights(j):
                sp.wait_ge(wt_lo["gate"], G * j + G)
                sp.dma_start(raw_slot("down"), down_j[j]).then_inc(raw_loaded["down"], 16)

            def next_weights(j, cols):
                sp.wait_ge(wt_lo["up"], G * j + G)
                sp.dma_start(raw_slot("up"), up_k[:, :, cols]).then_inc(raw_loaded["up"], 16)
                sp.wait_ge(wt_lo["down"], G * j + G)
                sp.dma_start(raw_slot("gate"), gate_k[:, :, cols]).then_inc(raw_loaded["gate"], 16)

            with sp.Fori(0, NJ - 1) as j:
                down_weights_dyn = down_j[bass.ds(j, 1)].rearrange("a p r d -> (a p) r d")
                sp.wait_ge(wt_lo["gate"], j * G + G)
                sp.dma_start(raw_slot("down"), down_weights_dyn).then_inc(raw_loaded["down"], 16)
                next_weights(j, bass.ds(j * (G * P) + G * P, G * P))
            down_weights(NJ - 1)
            for c in range(NCH):
                for t in range(TC):
                    tile = TC * c + t
                    sp.wait_ge(added, NT * (NJ - 1) + tile + 1)
                    sp.dma_start(out_tiles[tile], acc[:, tile, :]).then_inc(out_stored, 16)
            sp.wait_ge(out_stored, 16 * NT)

        @block.gpsimd
        def _(pool):
            nc.gpsimd.memset(ident[:], 0.0).then_inc(pool_step, 1)
            nc.gpsimd.memset(causal[:], 0.0).then_inc(pool_step, 1)
            nc.gpsimd.memset(neg_half[:], -0.5).then_inc(pool_step, 1)
            pool.wait_ge(pool_step, 3)
            nc.gpsimd.affine_select(out=ident[:], in_=ident[:], compare_op=ALU.not_equal, fill=1.0, base=0,
                                    pattern=[[-1, P]], channel_multiplier=1).then_inc(consts_ready, 1)
            nc.gpsimd.affine_select(out=causal[:], in_=causal[:], compare_op=ALU.is_ge, fill=MASKED, base=0,
                                    pattern=[[-1, P]], channel_multiplier=1).then_inc(consts_ready, 1)
            norms = 0
            for kind, n in steps:
                if kind in ("x_norm", "x_affine"):
                    pool.wait_ge(stats_ready, norms + 1)
                    if norms:
                        pool.wait_ge(x_ready, norms)
                    nc.gpsimd.tensor_scalar(var_eps[:], mean_var[:, :, 1], EPS, None, ALU.add).then_inc(pool_step, 1)
                    pool.wait_ge(pool_step, 4 + norms)
                    nc.gpsimd.tensor_tensor(rstd[:], var_eps[:], neg_half[:], ALU.pow).then_inc(rstd_ready, 1)
                    norms += 1

            def lo_half(m, r, j):
                pool.wait_ge(wt_hi[m], j * G + (r + 1))
                nc.gpsimd.tensor_tensor(piece(m, r, weight_lo[m]), raw_piece(m, r), piece(m, r, weight_hi[m]).bitcast(F32),
                                        ALU.subtract).then_inc(wt_lo[m], 1)

            for r in range(G):
                lo_half("gate", r, 0)
                lo_half("up", r, 0)
            with pool.Fori(0, NJ - 1) as j:
                for r in range(G):
                    lo_half("down", r, j)
                for r in range(G):
                    lo_half("gate", r, j + 1)
                    lo_half("up", r, j + 1)
            for r in range(G):
                lo_half("down", r, NJ - 1)

        @block.tensor
        def _(pe):
            def three(dst, pairs, **flags):
                for n, ((l_hi, l_lo), (r_hi, r_lo)) in enumerate(pairs):
                    pe.matmul(dst, l_hi, r_hi, start=(n == 0 and flags.get("first", True)), stop=False)
                    pe.matmul(dst, l_hi, r_lo, start=False, stop=False)
                    last = pe.matmul(dst, l_lo, r_hi, start=False, stop=(n == len(pairs) - 1 and flags.get("last", True)))
                return last

            def turn(no, dst_bank, blocks):
                if no >= TURN_RING:
                    pe.wait_ge(turn_free, no - TURN_RING + 1)
                for n, src in enumerate(blocks):
                    last = pe.transpose(dst_bank[:, n * P:(n + 1) * P], src, ident[:])
                last.then_inc(turn_full, 1)

            def bank_of_product(no):
                if no >= PROD_RING:
                    pe.wait_ge(prod_free, no - PROD_RING + 1)
                return prod_bank[no % PROD_RING]

            def cols(t_hi, t_lo, k, a, b):
                return t_hi[:, k, a:b], t_lo[:, k, a:b]

            def weight_product(kind, lhs, rhs):
                for h in range(KT):
                    no = prod_no[kind, 0, h]
                    three(bank_of_product(no)[:], [(cols(*lhs, k, h * P, (h + 1) * P), cols(*rhs, k, 0, W)) for k in range(KT)]
                          ).then_inc(prod_full, 1)

            pe.wait_ge(consts_ready, 2)
            norms = 0
            for kind, n in steps:
                if kind == "x_norm":
                    norms += 1
                    pe.wait_ge(x_ready, norms)
                    for k in range(KT):
                        no = turn_no[kind, n, k]
                        turn(no, turn_bank[no % TURN_RING], [xw[:, t, k * P:(k + 1) * P] for t in range(TC)])
                elif kind == "x_affine":
                    norms += 1
                    pe.wait_ge(x_ready, norms)
                    for k in range(KT):
                        no = turn_no[kind, n, k]
                        turn(no, turn_bank[no % TURN_RING], [xw[:, t, k * P:(k + 1) * P] for t in range(TC)])
                elif kind == "w_turn":
                    pe.wait_ge(w_loaded[n], 16)
                    for k in range(KT):
                        no = turn_no[kind, n, k]
                        turn(no, turn_bank[no % TURN_RING], [w_raw[n][:, h, k * P:(k + 1) * P] for h in range(KT)])
                elif kind == "qk_weight":
                    pe.wait_ge(turn_free, turn_no["w_turn", 1, KT - 1] + 1)
                    weight_product(kind, turned[0], turned[1])
                elif kind == "vo_weight":
                    pe.wait_ge(turn_free, turn_no["w_turn", 2, KT - 1] + 1)
                    pe.wait_ge(wo_ready, 1)
                    weight_product(kind, turned[2], (wo_hi, wo_lo))
                elif kind == "z":
                    pe.wait_ge(prod_free, prod_no["qk_weight", 0, KT - 1] + 1)
                    pe.wait_ge(turn_free, turn_no["x_affine", n, KT - 1] + 1)
                    for h in range(KT):
                        no = prod_no[kind, n, h]
                        three(bank_of_product(no)[:], [(cols(mu_hi, mu_lo, k, h * P, (h + 1) * P),
                                                        cols(xT_hi, xT_lo, k, n * W, (n + 1) * W)) for k in range(KT)]
                              ).then_inc(prod_full, 1)
                elif kind == "v":
                    pe.wait_ge(prod_free, prod_no["vo_weight", 0, KT - 1] + 1)
                    for t in range(TC):
                        no = prod_no[kind, n, t]
                        a = n * W + t * P
                        three(bank_of_product(no)[:], [(cols(xT_hi, xT_lo, k, a, a + P), cols(vo_hi, vo_lo, k, 0, W))
                                                       for k in range(KT)]).then_inc(prod_full, 1)
                elif kind == "scores":
                    a = n % TC * P
                    pe.wait_ge(prod_free, prod_no["z", n // TC, KT - 1] + 1)
                    for g, keys in enumerate(key_tiles(n)):
                        no = prod_no[kind, n, g]
                        width = len(keys) * P
                        three(bank_of_product(no)[:, 0:width],
                              [(cols(zg_hi, zg_lo, k, a, a + P), cols(xT_hi, xT_lo, k, g * W, g * W + width)) for k in range(KT)]
                              ).then_inc(prod_full, 1)
                elif kind == "attend":
                    groups = key_tiles(n)
                    pe.wait_ge(exp_ready, n + 1)
                    if n >= OUT_RING:
                        pe.wait_ge(rows_ready, n - OUT_RING + 1)
                    pe.wait_ge(prod_free, prod_no["v", n // TC, TC - 1] + 1)
                    for g in range(len(groups) + 1):
                        if g < len(groups):
                            no = turn_no[kind, n, g]
                            turn(no, turn_bank[no % TURN_RING], [raw[:, n % 2, t * P:(t + 1) * P] for t in groups[g]])
                        if g >= 1:
                            keys, slot = groups[g - 1], group_no[n, g - 1] % PT_RING
                            pe.wait_ge(turn_free, turn_no[kind, n, g - 1] + 1)
                            three(o_bank[n % OUT_RING][:],
                                  [((pT_hi[:, slot, b * P:(b + 1) * P], pT_lo[:, slot, b * P:(b + 1) * P]),
                                    (v_hi[:, t, :], v_lo[:, t, :])) for b, t in enumerate(keys)],
                                  first=(g == 1), last=(g == len(groups))).then_inc(group_attended, 1)

            pe.wait_ge(prod_free, len(prod_no))
            pe.wait_ge(turn_free, len(turn_no))

            def gate_up(j, c):
                for r in range(G):
                    fill = j * (NCH * G) + (c * G + r)
                    if type(j) is not int or c or j or r >= 2:
                        pe.wait_ge(hid_ready, fill - 1)
                    for m, banks, full in (("gate", gate_bank, gate_full), ("up", up_bank, up_full)):
                        if c == 0:
                            pe.wait_ge(wt_lo[m], j * G + (r + 1))
                        wh, wl = weight_hi[m], weight_lo[m]
                        for k in range(KT):
                            lhs_hi, lhs_lo = wh[:, k, r * P:(r + 1) * P], wl[:, k, r * P:(r + 1) * P]
                            rhs_hi, rhs_lo = cols(xT_hi, xT_lo, k, c * W, (c + 1) * W)
                            pe.matmul(banks[r % 2][:], lhs_hi, rhs_hi, start=(k == 0), stop=False)
                            pe.matmul(banks[r % 2][:], lhs_hi, rhs_lo, start=False, stop=False)
                            last = pe.matmul(banks[r % 2][:], lhs_lo, rhs_hi, start=False, stop=(k == KT - 1))
                        last.then_inc(full, 1)

            def down(j, c, peeled_first=False):
                if c == 0:
                    pe.wait_ge(wt_lo["down"], j * G + G)
                for t in range(TC):
                    if not peeled_first:
                        pe.wait_ge(added, j * NT + (c * TC + t) - (TC - 1))
                    for r in range(G):
                        if t == 0:
                            pe.wait_ge(hs_ready, j * (NCH * G) + (c * G + r + 1))
                        s_hi, s_lo = hs_hi[:, r, t * P:(t + 1) * P], hs_lo[:, r, t * P:(t + 1) * P]
                        pe.matmul(down_bank[t][:], s_hi, dw_hi[:, r, :], start=(r == 0), stop=False)
                        pe.matmul(down_bank[t][:], s_hi, dw_lo[:, r, :], start=False, stop=False)
                        last = pe.matmul(down_bank[t][:], s_lo, dw_hi[:, r, :], start=False, stop=(r == G - 1))
                    last.then_inc(down_full, 1)

            def block_of_weights(j, last):
                for c in range(1, NCH):
                    if type(j) is int and j == 0:
                        pe.wait_ge(xnT_loaded[c], 32)
                    gate_up(j, c)
                    down(j, c - 1, peeled_first=(type(j) is int and j == 0 and c == 1))
                if not last:
                    gate_up(j + 1, 0)
                down(j, NCH - 1)

            pe.wait_ge(xnT_loaded[0], 32)
            gate_up(0, 0)
            pe.wait_ge(rows_ready, NT)
            block_of_weights(0, False)
            with pe.Fori(1, NJ - 1) as j:
                block_of_weights(j, False)
            block_of_weights(NJ - 1, True)

        @block.scalar
        def _(act):
            for kind, n in steps:
                if kind in ("x_norm", "w_turn", "x_affine"):
                    for k in range(KT):
                        no = turn_no[kind, n, k]
                        src = turn_bank[no % TURN_RING]
                        if kind == "w_turn":
                            dst = turned[n][0][:, k, :]
                            act.wait_ge(turn_full, no + 1)
                        elif kind == "x_norm":
                            dst = stage_hi[:, k % 2, :]
                            act.wait_ge(turn_full, no + 1)
                            if (n, k) >= (0, 2):
                                act.wait_ge(xnT_stored[k % 2], 32 * ((n * KT + k) // 2))
                        else:
                            dst = xT_hi[:, k, n * W:(n + 1) * W]
                            act.wait_ge(turn_affine, n * KT + k + 1)
                        nc.scalar.copy(dst, src[:]).then_inc(turn_hi, 1)
                    if (kind, n) == ("w_turn", 2):
                        act.wait_ge(wo_loaded, 16)
                        nc.scalar.copy(wo_hi, wo_raw[:]).then_inc(wo_hi_ready, 1)
                elif kind in ("qk_weight", "vo_weight", "z", "v"):
                    for k in range(KT):
                        no = prod_no[kind, n, k]
                        dst = {"qk_weight": mu_hi, "vo_weight": vo_hi, "z": zg_hi, "v": v_hi[:, n * TC:(n + 1) * TC, :]}[kind]
                        act.wait_ge(prod_full, no + 1)
                        nc.scalar.copy(dst[:, k, :], prod_bank[no % PROD_RING][:]).then_inc(prod_hi, 1)
                elif kind == "scores":
                    act.wait_ge(max_ready, n + 1)
                    probs = raw[:, n % 2, 0:(n + 1) * P]
                    nc.scalar.activation(probs, probs, ACT.Exp, bias=neg_max[:, n % 2:n % 2 + 1], scale=SCALE,
                                         accum_out=row_sum[:, n:n + 1]).then_inc(exp_ready, 1)
                elif kind == "attend":
                    for g, keys in enumerate(key_tiles(n)):
                        no, gno = turn_no[kind, n, g], group_no[n, g]
                        act.wait_ge(turn_full, no + 1)
                        if gno >= PT_RING:
                            act.wait_ge(group_attended, gno - PT_RING + 1)
                        width = len(keys) * P
                        nc.scalar.copy(pT_hi[:, gno % PT_RING, 0:width], turn_bank[no % TURN_RING][:, 0:width]).then_inc(turn_hi, 1)

            def hi_half(m, r, j):
                nc.scalar.copy(piece(m, r, weight_hi[m]), raw_piece(m, r)).then_inc(wt_hi[m], 1)

            def chunk(j, c, split_next, split_down):
                first = type(j) is int and j == 0 and c == 0
                for r in range(G + 1):
                    fill = j * (NCH * G) + (c * G + r)
                    if r < G:
                        act.wait_ge(gate_full, fill + 1)
                        if not (first and r < 2):
                            act.wait_ge(hid_ready, fill - 1)
                        nc.scalar.activation(rows[:, r % 2, :], gate_bank[r % 2][:], ACT.Silu).then_inc(silu_ready, 1)
                    if split_down and r == 0:
                        act.wait_ge(raw_loaded["down"], j * 16 + 16)
                        if not (type(j) is int and j == 0):
                            act.wait_ge(down_full, j * NT)
                        for q in range(G):
                            hi_half("down", q, j)
                    if r >= 1:
                        act.wait_ge(hid_ready, fill)
                        if r == 1 and not first:
                            act.wait_ge(pick_step, (j * NCH + c) * PICK - (PICK - 4))
                        nc.scalar.activation(mag[:, r - 1, :], hid[:, r - 1, :], ACT.Abs).then_inc(mag_ready, 1)
                        if split_next:
                            for m, full in (("gate", gate_full), ("up", up_full)):
                                if r == 1:
                                    act.wait_ge(raw_loaded[m], j * 16 + 32)
                                act.wait_ge(full, fill)
                                hi_half(m, r - 1, j + 1)
                if not first:
                    act.wait_ge(down_full, (j * NCH + c) * TC)
                for r in range(G):
                    act.wait_ge(picked, j * (NCH * G) + (c * G + r + 1))
                    nc.scalar.copy(hs_hi[:, r, :], hid[:, r, :]).then_inc(hs_hi_ready, 1)

            def block_of_weights(j, last):
                for c in range(1, NCH):
                    chunk(j, c, split_next=(c == NCH - 1 and not last), split_down=(c == 1))
                if not last:
                    chunk(j + 1, 0, False, False)

            act.wait_ge(prod_full, len(prod_no))
            for m in ("gate", "up"):
                act.wait_ge(raw_loaded[m], 16)
                for r in range(G):
                    hi_half(m, r, 0)
            act.wait_ge(resid_stored, 16 * NT)
            chunk(0, 0, False, False)
            block_of_weights(0, False)
            with act.Fori(1, NJ - 1) as j:
                block_of_weights(j, False)
            block_of_weights(NJ - 1, True)

        @block.vector
        def _(dve):
            made = [0]

            def step(ins):
                made[0] += 1
                ins.then_inc(vec_step, 1)
                return made[0]

            def statistics():
                for t in range(TC):
                    n = step(nc.vector.bn_stats(stats[:, t, :], xw[:, t, :]))
                dve.wait_ge(vec_step, n)
                for t in range(TC):
                    last = nc.vector.bn_aggr(mean_var[:, t, :], stats[:, t, :])
                last.then_inc(stats_ready, 1)

            def normalise(norms):
                dve.wait_ge(stats_ready, norms)
                dve.wait_ge(rstd_ready, norms)
                for t in range(TC):
                    last = nc.vector.tensor_scalar(xw[:, t, :], xw[:, t, :], mean_var[:, t, 0:1], rstd[:, t:t + 1],
                                                   ALU.subtract, ALU.mult)
                last.then_inc(x_ready, 1)

            def lo_of_turned(kind, n, k, dst_lo, src_hi):
                no = turn_no[kind, n, k]
                dve.wait_ge(turn_hi, turned_hi_no[kind, n, k] + 1)
                width = src_hi.shape[-1]
                nc.vector.tensor_tensor(dst_lo, turn_bank[no % TURN_RING][:, 0:width], src_hi.bitcast(F32),
                                        ALU.subtract).then_inc(turn_free, 1)

            norms = 0
            for kind, n in steps:
                if kind == "x_norm":
                    dve.wait_ge(x_loaded, 16 * (n + 1))
                    norms += 1
                    statistics()
                    normalise(norms)
                    own = slice(n * TC, (n + 1) * TC)
                    nc.vector.tensor_scalar(one_rstd[:, own], rstd[:], 1.0, None, ALU.add)
                    nc.vector.scalar_tensor_tensor(out=neg_mean_rstd[:, own], in0=mean_var[:, :, 0], scalar=-1.0, in1=rstd[:],
                                                   op0=ALU.mult, op1=ALU.mult)
                    for k in range(KT):
                        if (n, k) >= (0, 2):
                            dve.wait_ge(xnT_stored[k % 2], 32 * ((n * KT + k) // 2))
                        lo_of_turned(kind, n, k, stage_lo[:, k % 2, :], stage_hi[:, k % 2, :])
                elif kind == "x_affine":
                    norms += 1
                    dve.wait_ge(x_ready, norms - 1)
                    statistics()
                    dve.wait_ge(turn_full, turn_no["x_norm", n, KT - 1] + 1)
                    normalise(norms)
                    if n == 0:
                        dve.wait_ge(affine_loaded, 32)
                    for k in range(KT + 1):
                        if k < KT:
                            no = turn_no[kind, n, k]
                            dve.wait_ge(turn_full, no + 1)
                            b = turn_bank[no % TURN_RING]
                            nc.vector.tensor_scalar(b[:], b[:], gamma_t[:, k:k + 1], beta_t[:, k:k + 1], ALU.mult,
                                                    ALU.add).then_inc(turn_affine, 1)
                        if k >= 1:
                            own = slice(n * W, (n + 1) * W)
                            lo_of_turned(kind, n, k - 1, xT_lo[:, k - 1, own], xT_hi[:, k - 1, own])
                elif kind == "w_turn":
                    for k in range(KT):
                        lo_of_turned(kind, n, k, turned[n][1][:, k, :], turned[n][0][:, k, :])
                    if n == 2:
                        dve.wait_ge(wo_hi_ready, 1)
                        nc.vector.tensor_tensor(wo_lo, wo_raw[:], wo_hi.bitcast(F32), ALU.subtract).then_inc(wo_ready, 1)
                elif kind in ("qk_weight", "vo_weight", "z", "v"):
                    if (kind, n) == ("v", NCH - 1):
                        for stored in xnT_stored:
                            dve.wait_ge(stored, 16 * KT * NCH)
                    for k in range(KT):
                        no = prod_no[kind, n, k]
                        dst_hi, dst_lo = {"qk_weight": (mu_hi, mu_lo), "vo_weight": (vo_hi, vo_lo), "z": (zg_hi, zg_lo),
                                          "v": (v_hi[:, n * TC:(n + 1) * TC, :], v_lo[:, n * TC:(n + 1) * TC, :])}[kind]
                        dve.wait_ge(prod_hi, split_no[kind, n, k] + 1)
                        nc.vector.tensor_tensor(dst_lo[:, k, :], prod_bank[no % PROD_RING][:], dst_hi[:, k, :].bitcast(F32),
                                                ALU.subtract).then_inc(prod_free, 1)
                elif kind == "scores":
                    groups, slot, parts = key_tiles(n), n % 2, 0
                    if n >= 2:
                        dve.wait_ge(exp_ready, n - 1)
                    for g, keys in enumerate(groups):
                        no = prod_no[kind, n, g]
                        src = prod_bank[no % PROD_RING]
                        dve.wait_ge(prod_full, no + 1)
                        full = len(keys) * P - (P if g == len(groups) - 1 else 0)
                        if full:
                            last = nc.vector.tensor_scalar(raw[:, slot, g * W:g * W + full], src[:, 0:full], 1.0, None, ALU.mult,
                                                           ALU.max, accum_out=part_max[:, slot, parts:parts + 1])
                            parts += 1
                            if g < len(groups) - 1:
                                last.then_inc(prod_free, 1)
                    diagonal = raw[:, slot, n * P:(n + 1) * P]
                    nc.vector.tensor_tensor(diagonal, src[:, full:full + P], causal[:], ALU.add).then_inc(prod_free, 1)
                    dve.wait_ge(prod_free, prod_no[kind, n, len(groups) - 1] + 1)
                    done = step(nc.vector.reduce_max(part_max[:, slot, parts:parts + 1], diagonal, AX.X))
                    dve.wait_ge(vec_step, done)
                    done = step(nc.vector.reduce_max(row_max[:, slot:slot + 1], part_max[:, slot, 0:parts + 1], AX.X))
                    dve.wait_ge(vec_step, done)
                    nc.vector.tensor_scalar(neg_max[:, slot:slot + 1], row_max[:, slot:slot + 1], -SCALE, None,
                                            ALU.mult).then_inc(max_ready, 1)
                elif kind == "attend":
                    slot = n % 2
                    for g, keys in enumerate(key_tiles(n)):
                        width = len(keys) * P
                        gno = group_no[n, g]
                        lo_of_turned(kind, n, g, pT_lo[:, gno % PT_RING, 0:width], pT_hi[:, gno % PT_RING, 0:width])
                    dve.wait_ge(rows_loaded[slot], 16 * (n // 2 + 1))
                    a = step(nc.vector.tensor_scalar(rows[:, slot, :], rows[:, slot, :], one_rstd[:, n:n + 1],
                                                     neg_mean_rstd[:, n:n + 1], ALU.mult, ALU.add))
                    done = step(nc.vector.reciprocal(inv_sum[:, n:n + 1], row_sum[:, n:n + 1]))
                    dve.wait_ge(vec_step, done)
                    dve.wait_ge(group_attended, group_no[n, len(key_tiles(n)) - 1] + 1)
                    nc.vector.scalar_tensor_tensor(out=rows[:, slot, :], in0=o_bank[n % OUT_RING][:], scalar=inv_sum[:, n:n + 1],
                                                   in1=rows[:, slot, :], op0=ALU.mult, op1=ALU.add).then_inc(rows_ready, 1)

            def add_down(j, c):
                for t in range(TC):
                    tile = c * TC + t
                    dve.wait_ge(down_full, j * NT + (tile + 1))
                    nc.vector.tensor_tensor(acc[:, tile, :], down_bank[t][:], acc[:, tile, :], ALU.add).then_inc(added, 1)

            def chunk(j, c, before):
                base = j * (NCH * G) + c * G
                if before is not None:
                    dve.wait_ge(hs_ready, base)
                for r in range(G):
                    dve.wait_ge(silu_ready, base + (r + 1))
                    dve.wait_ge(up_full, base + (r + 1))
                    nc.vector.tensor_tensor(hid[:, r, :], rows[:, r % 2, :], up_bank[r % 2][:], ALU.mult).then_inc(hid_ready, 1)
                dve.wait_ge(mag_ready, base + G)
                picks = (j * NCH + c) * PICK
                nc.vector.tensor_tensor(beats_a[:], mag[:, 0:G:2, :], mag[:, 1:G:2, :], ALU.is_ge).then_inc(pick_step, 1)
                nc.vector.tensor_tensor(beats_b[:], mag[:, 0:2, :], mag[:, 2:4, :], ALU.is_ge).then_inc(pick_step, 1)
                nc.vector.tensor_tensor(beats_c[:, 0, :], mag[:, 0, :], mag[:, 3, :], ALU.is_ge).then_inc(pick_step, 1)
                nc.vector.tensor_tensor(beats_c[:, 1, :], mag[:, 1, :], mag[:, 2, :], ALU.is_ge).then_inc(pick_step, 1)
                dve.wait_ge(pick_step, picks + 4)
                nc.vector.tensor_tensor(pair_sum[:], beats_b[:], beats_c[:], ALU.add).then_inc(pick_step, 1)
                dve.wait_ge(pick_step, picks + 5)
                nc.vector.tensor_tensor(beats_b[:, 0, :], beats_b[:, 0, :], beats_c[:, 1, :], ALU.add).then_inc(pick_step, 1)
                nc.vector.tensor_tensor(beats_b[:, 1, :], beats_b[:, 1, :], beats_c[:, 0, :], ALU.add).then_inc(pick_step, 1)
                dve.wait_ge(pick_step, picks + 7)
                nc.vector.tensor_tensor(pair_sum[:, 0, :], pair_sum[:, 0, :], beats_a[:, 0, :], ALU.add).then_inc(pick_step, 1)
                nc.vector.tensor_tensor(pair_sum[:, 1, :], pair_sum[:, 1, :], beats_a[:, 0, :], ALU.subtract).then_inc(pick_step, 1)
                nc.vector.tensor_tensor(beats_b[:, 0, :], beats_a[:, 1, :], beats_b[:, 0, :], ALU.subtract).then_inc(pick_step, 1)
                nc.vector.tensor_tensor(beats_b[:, 1, :], beats_b[:, 1, :], beats_a[:, 1, :], ALU.add).then_inc(pick_step, 1)
                dve.wait_ge(pick_step, picks + PICK)
                rules = ((pair_sum[:, 0, :], 2.0, ALU.is_ge), (pair_sum[:, 1, :], 1.0, ALU.is_ge),
                         (beats_b[:, 0, :], 0.0, ALU.is_ge), (beats_b[:, 1, :], 1.0, ALU.is_le))
                for r, (wins, bound, rule) in enumerate(rules):
                    nc.vector.scalar_tensor_tensor(out=hid[:, r, :], in0=wins, scalar=bound, in1=hid[:, r, :], op0=rule,
                                                   op1=ALU.mult).then_inc(picked, 1)
                if before is not None:
                    add_down(*before)
                for r in range(G):
                    dve.wait_ge(hs_hi_ready, base + (r + 1))
                    nc.vector.tensor_tensor(hs_lo[:, r, :], hid[:, r, :], hs_hi[:, r, :].bitcast(F32), ALU.subtract).then_inc(hs_ready, 1)

            def block_of_weights(j, last):
                for c in range(1, NCH):
                    chunk(j, c, (j, c - 1))
                if not last:
                    chunk(j + 1, 0, (j, NCH - 1))
                else:
                    add_down(j, NCH - 1)

            chunk(0, 0, None)
            dve.wait_ge(acc_loaded, 16 * NCH)
            block_of_weights(0, False)
            with dve.Fori(1, NJ - 1) as j:
                block_of_weights(j, False)
            block_of_weights(NJ - 1, True)


INPUTS = ["L0_attn_x", "L0_attn_qkv", "L0_attn_o_proj", "L0_attn_gamma", "L0_attn_beta",
          "L0_ffn_w_gate", "L0_ffn_w_up", "L0_ffn_w_down"]


def kernel(**inputs):
    import numpy as np
    import concourse.bacc as bacc
    from concourse.bass_utils import run_bass_kernel_spmd

    nc = bacc.Bacc("TRN2", target_bir_lowering=False, num_devices=1)
    arrays, args = {}, []
    for name in INPUTS:
        a = np.asarray(inputs[name])
        if a.ndim == 1:
            a = a.reshape(-1, P).T
        a = np.ascontiguousarray(a)
        arrays[name] = a
        args.append(nc.dram_tensor(name, a.shape, mybir.dt.from_np(a.dtype), kind="ExternalInput").ap())
    shape = arrays["L0_attn_x"].shape
    result = nc.dram_tensor("result", shape, F32, kind="ExternalOutput").ap()
    attention_ffn(nc, *args, result)
    r = run_bass_kernel_spmd(nc, [arrays], core_ids=[0])
    return r.results[0]["result"]
```

```python
from contextlib import ExitStack

import concourse.bass as bass
from concourse import mybir

ALU = mybir.AluOpType
ACT = mybir.ActivationFunctionType
AX = mybir.AxisListType
F32 = mybir.dt.float32
F32R = mybir.dt.float32r
BF16 = mybir.dt.bfloat16

P = 128
W = 512
EPS = 1e-5
MASKED = -3.0e38


def attention_ffn(nc, x, qkv_t, o_proj, gamma, beta, w_gate, w_up, w_down, out):
    _, S, D = x.shape
    I = w_gate.shape[1]
    KT = D // P
    NT = S // P
    NCH = S // W
    TC = W // P
    G = 4
    NJ = I // (G * P)
    SCALE = float(D) ** -0.5
    assert D == W and KT == TC == NCH == G and NJ >= 2

    x_chunks = x.rearrange("a (c t p) d -> (a c) p t d", t=TC, p=P)
    x_tiles = x.rearrange("a (n p) d -> (a n) p d", p=P)
    out_tiles = out.rearrange("a (n p) d -> (a n) p d", p=P)
    out_chunks = out.rearrange("a (c t p) d -> (a c) p t d", t=TC, p=P)
    qkv_tiles = qkv_t.rearrange("(m k p) n -> m k p n", k=KT, p=P)
    o_proj_tiles = o_proj.rearrange("(k p) n -> k p n", p=P)
    gate_k = w_gate.rearrange("(k p) i -> p k i", p=P)
    up_k = w_up.rearrange("(k p) i -> p k i", p=P)
    down_j = w_down.rearrange("(j p r) d -> j p r d", p=P, r=G)
    xnT_hi_dram = nc.dram_tensor("xnT_hi", (NCH, KT, P, W), F32, kind="Internal").ap()
    xnT_lo_dram = nc.dram_tensor("xnT_lo", (NCH, KT, P, W), F32, kind="Internal").ap()
    resid_dram = nc.dram_tensor("resid", (NT, P, D), F32, kind="Internal").ap()

    def fills(kind, n):
        return [(kind, n, k) for k in range(KT)]

    qk, vo = fills("qk_weight", 0), fills("vo_weight", 0)
    xn, xh_t, z, v = ([fills(kind, c) for c in range(NCH)] for kind in ("xn_turn", "xh_turn", "z", "v"))
    stats_of, scale_of, exp = ([(kind, n, 0) for n in range(NT)] for kind in ("x_stats", "x_scale", "exp"))
    steps = [step for k in range(KT) for step in (("split", 0, k), ("split", 1, k))] + [stats_of[0]]
    steps += [qk[0], *fills("split", 2), *fills("split", 3), qk[1], scale_of[0], qk[2], qk[3]]
    steps += [vo[0], vo[1], *xh_t[0][0:3], vo[2], xh_t[0][3], xn[0][0], vo[3], *xn[0][1:3], z[0][0], xn[0][3], *z[0][1:3]]
    steps += [stats_of[1], z[0][3], v[0][0], ("scores", 0, 0), exp[0], scale_of[1], *v[0][1:3], *xh_t[1][0:2]]
    before = {7: [z[2][0], stats_of[3], *z[2][1:4]]}
    between = {3: [*z[1][0:3], stats_of[2], z[1][3], v[1][1], scale_of[2]],
               7: [scale_of[3]],
               8: [xh_t[3][3]],
               11: [*z[3], *v[3]]}
    beside = {0: [v[0][3], exp[1], *xh_t[1][2:4]],
              1: [xn[1][0], exp[2], v[1][0], xn[1][1]],
              2: [xn[1][2], exp[3], xn[1][3]],
              3: [v[1][2], exp[4], *xh_t[2][0:2]],
              4: [v[1][3], exp[5], *xh_t[2][2:4], xn[2][0]],
              5: [xn[2][1], exp[6], xn[2][2]],
              6: [xn[2][3], exp[7]],
              7: [xh_t[3][0], exp[8], *xh_t[3][1:3]],
              8: [*v[2][0:2], xn[3][0]], 9: [v[2][2], xn[3][1]], 10: [v[2][3], *xn[3][2:4]],
              NT - 2: fills("first_split", "gate")}
    for i in range(NT):
        steps += [*before.get(i, []), ("head", i, 0), *between.get(i, [])]
        if i >= NT - TC:
            steps.append(("first_split", "up", i % TC))
        if i + 1 < NT:
            steps.append(("scores", i + 1, 0))
        steps += [*beside.get(i, []), ("attend", i, 0)]

    def key_tiles(i):
        return [range(g, min(g + TC, i + 1)) for g in range(0, i + 1, TC)]

    HEAD = 2
    turn_no, prod_no, split_no, group_no = {}, {}, {}, {}

    def groups_of(kind, i):
        ng = len(key_tiles(i))
        return range(0, min(HEAD, ng)) if kind == "head" else range(HEAD, ng)

    for kind, n, k in steps:
        if kind in ("xn_turn", "xh_turn"):
            turn_no[kind, n, k] = len(turn_no)
        elif kind in ("head", "attend"):
            for g in groups_of(kind, n):
                turn_no["probs", n, g] = len(turn_no)
                group_no[n, g] = len(group_no)
        elif kind == "scores":
            for g in range(len(key_tiles(n))):
                prod_no[kind, n, g] = len(prod_no)
        elif kind in ("qk_weight", "vo_weight", "z", "v"):
            prod_no[kind, n, k] = len(prod_no)
            split_no[kind, n, k] = len(split_no)
    PROD_RING, TURN_RING, PT_RING = 4, 3, 2

    with ExitStack() as ctx:
        def sem(name):
            return ctx.enter_context(nc.semaphore(name))

        def sb(name, shape, dt, where=ctx):
            return where.enter_context(nc.sbuf_tensor(name, shape, dt))

        bank = [ctx.enter_context(nc.psum_tensor(f"bank{b}", [P, W], F32)) for b in range(8)]
        prod_bank, turn_bank, o_bank = bank[0:4], bank[4:7], bank[7]
        gate_bank, up_bank, down_bank = bank[0:2], bank[2:4], bank[4:8]

        xT_hi, xT_lo = sb("xT_hi", [P, KT, S], F32R), sb("xT_lo", [P, KT, S], F32R)
        zg_hi, zg_lo = sb("zg_hi", [P, KT, W], F32R), sb("zg_lo", [P, KT, W], F32R)
        mu_hi, mu_lo = sb("mu_hi", [P, KT, W], F32R), sb("mu_lo", [P, KT, W], F32R)
        raw = sb("raw", [P, 2, G * W], F32)
        rows = sb("rows", [P, 2, W], F32)
        ident = sb("ident", [P, P], F32)
        causal = sb("causal", [P, P], F32)
        gamma_t, beta_t = sb("gamma_t", [P, KT], F32), sb("beta_t", [P, KT], F32)
        neg_half = sb("neg_half", [P, TC], F32)
        stats = sb("stats", [P, TC, 6], F32)
        mean_var = sb("mean_var", [P, TC, 2], F32)
        var_eps, rstd, rstd2 = (sb(n, [P, TC], F32) for n in ("var_eps", "rstd", "rstd2"))
        scaled_var, norm_var, norm_var_eps = (sb(n, [P, TC], F32) for n in ("scaled_var", "norm_var", "norm_var_eps"))
        one_rstd, neg_mean_rstd = sb("one_rstd", [P, NT], F32), sb("neg_mean_rstd", [P, NT], F32)
        part_max = sb("part_max", [P, 2, NCH + 1], F32)
        row_max, neg_max = sb("row_max", [P, 2], F32), sb("neg_max", [P, 2], F32)
        row_sum, inv_sum = sb("row_sum", [P, NT], F32), sb("inv_sum", [P, NT], F32)

        with ExitStack() as early:
            sb("pad_hi", [P, 2 * TC, W], F32, early)
            xh = sb("xh", [P, TC, D], F32, early)
            xw = sb("xw", [P, TC, D], F32, early)
            sb("pad_lo", [P, 3 * TC, W], F32, early)
            stage_hi, stage_lo = sb("stage_hi", [P, 2, W], F32R, early), sb("stage_lo", [P, 2, W], F32R, early)
        with ExitStack() as attention:
            v_hi, v_lo = sb("v_hi", [P, NT, D], F32R, attention), sb("v_lo", [P, NT, D], F32R, attention)
            pT_hi, pT_lo = sb("pT_hi", [P, PT_RING, W], F32R, attention), sb("pT_lo", [P, PT_RING, W], F32R, attention)
            vo_hi, vo_lo = sb("vo_hi", [P, KT, W], F32R, attention), sb("vo_lo", [P, KT, W], F32R, attention)
        with ExitStack() as ends:
            sb("pad_ends", [P, 2 * NT * D + 2 * PT_RING * W], F32, ends)
            first_raw = sb("first_raw", [P, 2, G * W], F32, ends)
        with ExitStack() as ffn:
            acc = sb("acc", [P, NT, D], F32, ffn)
            dw_hi, dw_lo = sb("dw_hi", [P, G, D], F32R, ffn), sb("dw_lo", [P, G, D], F32R, ffn)
            hs_hi, hs_lo = sb("hs_hi", [P, G, W], F32R, ffn), sb("hs_lo", [P, G, W], F32R, ffn)
            hid = sb("hid", [P, G, W], F32, ffn)
            mag = sb("mag", [P, G, W], F32, ffn)
            beats_a, beats_b = sb("beats_a", [P, 2, W], BF16, ffn), sb("beats_b", [P, 2, W], BF16, ffn)
            beats_c, pair_sum = sb("beats_c", [P, 2, W], BF16, ffn), sb("pair_sum", [P, 2, W], BF16, ffn)
        turned = [(xT_hi[:, :, 2 * W:3 * W], xT_lo[:, :, 2 * W:3 * W]), (xT_hi[:, :, 3 * W:4 * W], xT_lo[:, :, 3 * W:4 * W]),
                  (v_hi[:, TC:2 * TC, :], v_lo[:, TC:2 * TC, :]), (v_hi[:, 0:TC, :], v_lo[:, 0:TC, :])]

        x_loaded, affine_loaded = sem("x_loaded"), sem("affine_loaded")
        w_loaded = [[sem(f"wq_loaded{k}") for k in range(KT)], [sem(f"wk_loaded{k}") for k in range(KT)],
                    [sem(f"wv_loaded{k}") for k in range(KT)], [sem(f"wo_loaded{k}") for k in range(KT)]]
        w_hi_ready = [sem(f"{m}_hi_ready") for m in ("wq", "wk", "wv", "wo")]
        w_ready = [sem(f"{m}_ready") for m in ("wq", "wk", "wv", "wo")]
        resid_stored = sem("resid_stored")
        xnT_stored = [sem("xnT_stored0"), sem("xnT_stored1")]
        rows_loaded = [sem("rows_loaded0"), sem("rows_loaded1")]
        consts_ready, pool_step = sem("consts_ready"), sem("pool_step")
        stats_ready, rstd_ready, rstd2_ready = sem("stats_ready"), sem("rstd_ready"), sem("rstd2_ready")
        xn_ready, xh_ready = sem("xn_ready"), sem("xh_ready")
        turn_full, turn_affine, turn_hi, turn_free = sem("turn_full"), sem("turn_affine"), sem("turn_hi"), sem("turn_free")
        prod_full, prod_hi, prod_free = sem("prod_full"), sem("prod_hi"), sem("prod_free")
        vec_step = sem("vec_step")
        max_ready, exp_ready, group_attended, rows_ready = sem("max_ready"), sem("exp_ready"), sem("group_attended"), sem("rows_ready")
        raw_loaded = {m: sem(f"{m}_raw_loaded") for m in ("gate", "up", "down")}
        wt_hi = {m: sem(f"{m}_hi_ready") for m in ("gate", "up", "down")}
        wt_lo = {m: sem(f"{m}_lo_ready") for m in ("gate", "up", "down")}
        xnT_loaded = [sem(f"xnT_loaded{c}") for c in range(NCH)]
        acc_loaded = sem("acc_loaded")
        gate_full, up_full, silu_ready, hid_ready, mag_ready = (sem(n) for n in ("gate_full", "up_full", "silu_ready", "hid_ready", "mag_ready"))
        pick_step, picked, hs_hi_ready, hs_ready = (sem(n) for n in ("pick_step", "picked", "hs_hi_ready", "hs_ready"))
        down_full, added, out_stored = sem("down_full"), sem("added"), sem("out_stored")
        PICK = 11

        last_bank = gate_bank + up_bank
        last_units = xT_hi[:, :, 0:W], xT_lo[:, :, 0:W]

        block = ctx.enter_context(nc.Block())

        def raw_slot(m):
            return raw[:, 1 if m == "up" else 0, :].rearrange("p (k n) -> p k n", k=G)

        def first_slot(m):
            return first_raw[:, 1 if m == "up" else 0, :].rearrange("p (k n) -> p k n", k=G)

        def w_raw(m, k):
            return (raw if m < 2 else first_raw)[:, m % 2, k * W:(k + 1) * W]

        weight_hi = {"gate": zg_hi, "up": mu_hi, "down": dw_hi}
        weight_lo = {"gate": zg_lo, "up": mu_lo, "down": dw_lo}

        def piece(m, r, t):
            return t[:, :, r * P:(r + 1) * P] if m != "down" else t[:, r, :]

        def raw_piece(m, r, slot):
            return slot.rearrange("p k (g r) -> p k g r", r=G)[:, :, :, r] if m != "down" else slot[:, r, :]

        last_turn = {i: turn_no["probs", i, len(key_tiles(i)) - 1] + 1 for i in range(NT)}

        @block.sync
        def _(sp):
            for k in range(KT):
                for m in (0, 1):
                    sp.dma_start(w_raw(m, k), qkv_tiles[m, k]).then_inc(w_loaded[m][k], 16)
            sp.dma_start(xw[:], x_chunks[0]).then_inc(x_loaded, 16)
            sp.dma_start(gamma_t[:], gamma).then_inc(affine_loaded, 16)
            sp.dma_start(beta_t[:], beta).then_inc(affine_loaded, 16)
            for k in range(KT):
                sp.dma_start(w_raw(2, k), qkv_tiles[2, k]).then_inc(w_loaded[2][k], 16)
            for k in range(KT):
                sp.dma_start(w_raw(3, k), o_proj_tiles[k]).then_inc(w_loaded[3][k], 16)
            for kind, n, k in steps:
                if kind == "xn_turn":
                    sp.wait_ge(turn_free, turn_no[kind, n, k] + 1)
                    sp.dma_start(xnT_hi_dram[n, k], stage_hi[:, k % 2, :].bitcast(F32)).then_inc(xnT_stored[k % 2], 16)
                    sp.dma_start(xnT_lo_dram[n, k], stage_lo[:, k % 2, :].bitcast(F32)).then_inc(xnT_stored[k % 2], 16)
                elif kind == "scores":
                    if n >= 2:
                        sp.wait_ge(rows_ready, n - 1)
                        sp.dma_start(resid_dram[n - 2], rows[:, n % 2, :]).then_inc(resid_stored, 16)
                        sp.wait_ge(resid_stored, 16 * (n - 1))
                    sp.dma_start(rows[:, n % 2, :], x_tiles[n]).then_inc(rows_loaded[n % 2], 16)
                elif (kind, n, k) == ("v", NCH - 1, TC - 1):
                    sp.wait_ge(prod_full, prod_no[kind, n, k] + 1)
                    for m in (2, 3):
                        sp.wait_ge(w_ready[m], KT)
                    sp.dma_start(first_slot("up"), up_k[:, :, 0:G * P]).then_inc(raw_loaded["up"], 16)
                    sp.dma_start(first_slot("gate"), gate_k[:, :, 0:G * P]).then_inc(raw_loaded["gate"], 16)
            sp.wait_ge(prod_full, len(prod_no))
            for stored in xnT_stored:
                sp.wait_ge(stored, 16 * KT * NCH)
            for c in range(NCH):
                cols = slice(c * W, (c + 1) * W)
                sp.dma_start(xT_hi[:, :, cols].bitcast(F32), xnT_hi_dram[c].rearrange("k p s -> p k s")).then_inc(xnT_loaded[c], 16)
                sp.dma_start(xT_lo[:, :, cols].bitcast(F32), xnT_lo_dram[c].rearrange("k p s -> p k s")).then_inc(xnT_loaded[c], 16)
            sp.wait_ge(turn_full, last_turn[NT - 2])
            sp.dma_start(raw_slot("down"), down_j[0]).then_inc(raw_loaded["down"], 16)
            sp.wait_ge(turn_full, last_turn[NT - 1])
            sp.wait_ge(wt_lo["up"], G)
            sp.dma_start(raw_slot("up"), up_k[:, :, G * P:2 * G * P]).then_inc(raw_loaded["up"], 16)
            for i in (NT - 2, NT - 1):
                sp.wait_ge(rows_ready, i + 1)
                sp.dma_start(resid_dram[i], rows[:, i % 2, :]).then_inc(resid_stored, 16)
            sp.wait_ge(resid_stored, 16 * NT)
            for c in range(NCH):
                sp.dma_start(acc[:, TC * c:TC * (c + 1), :],
                             resid_dram[TC * c:TC * (c + 1)].rearrange("t p d -> p t d")).then_inc(acc_loaded, 16)

            def load_gate(j, cols):
                sp.wait_ge(wt_lo["down"], j * G)
                sp.dma_start(raw_slot("gate"), gate_k[:, :, cols]).then_inc(raw_loaded["gate"], 16)

            def load_down(j, block):
                sp.wait_ge(wt_lo["gate"], j * G + G)
                sp.dma_start(raw_slot("down"), block).then_inc(raw_loaded["down"], 16)

            def load_up(j, cols):
                sp.wait_ge(wt_lo["up"], j * G)
                sp.dma_start(raw_slot("up"), up_k[:, :, cols]).then_inc(raw_loaded["up"], 16)

            load_gate(1, slice(G * P, 2 * G * P))
            with sp.Fori(1, NJ - 1) as j:
                load_down(j, down_j[bass.ds(j, 1)].rearrange("a p r d -> (a p) r d"))
                load_up(j + 1, bass.ds(j * (G * P) + G * P, G * P))
                load_gate(j + 1, bass.ds(j * (G * P) + G * P, G * P))
            load_down(NJ - 1, down_j[NJ - 1])
            for c in range(NCH):
                for t in range(TC):
                    tile = TC * c + t
                    sp.wait_ge(added, NT * (NJ - 1) + tile + 1)
                    sp.dma_start(out_tiles[tile], acc[:, tile, :]).then_inc(out_stored, 16)
            sp.wait_ge(out_stored, 16 * NT)

        @block.gpsimd
        def _(pool):
            nc.gpsimd.memset(ident[:], 0.0).then_inc(pool_step, 1)
            nc.gpsimd.memset(causal[:], 0.0).then_inc(pool_step, 1)
            nc.gpsimd.memset(neg_half[:], -0.5).then_inc(pool_step, 1)
            pool.wait_ge(pool_step, 3)
            nc.gpsimd.affine_select(out=ident[:], in_=ident[:], compare_op=ALU.not_equal, fill=1.0, base=0,
                                    pattern=[[-1, P]], channel_multiplier=1).then_inc(consts_ready, 1)
            nc.gpsimd.affine_select(out=causal[:], in_=causal[:], compare_op=ALU.is_ge, fill=MASKED, base=0,
                                    pattern=[[-1, P]], channel_multiplier=1).then_inc(consts_ready, 1)
            done = 3

            def small(ins):
                nonlocal done
                done += 1
                ins.then_inc(pool_step, 1)
                pool.wait_ge(pool_step, done)

            def lo_half(m, r, j, slot):
                pool.wait_ge(wt_hi[m], j * G + (r + 1))
                nc.gpsimd.tensor_tensor(piece(m, r, weight_lo[m]), raw_piece(m, r, slot), piece(m, r, weight_hi[m]).bitcast(F32),
                                        ALU.subtract).then_inc(wt_lo[m], 1)

            for kind, n, k in steps:
                if kind == "x_stats":
                    pool.wait_ge(stats_ready, n + 1)
                    if n:
                        pool.wait_ge(xh_ready, n)
                    var = mean_var[:, :, 1]
                    small(nc.gpsimd.tensor_scalar(var_eps[:], var, EPS, None, ALU.add))
                    nc.gpsimd.tensor_tensor(rstd[:], var_eps[:], neg_half[:], ALU.pow).then_inc(rstd_ready, 1)
                    pool.wait_ge(rstd_ready, n + 1)
                    small(nc.gpsimd.tensor_tensor(scaled_var[:], var, rstd[:], ALU.mult))
                    small(nc.gpsimd.tensor_tensor(norm_var[:], scaled_var[:], rstd[:], ALU.mult))
                    small(nc.gpsimd.tensor_scalar(norm_var_eps[:], norm_var[:], EPS, None, ALU.add))
                    nc.gpsimd.tensor_tensor(rstd2[:], norm_var_eps[:], neg_half[:], ALU.pow).then_inc(rstd2_ready, 1)
                elif kind == "first_split":
                    lo_half(n, k, 0, first_slot(n))
            with pool.Fori(0, NJ - 1) as j:
                for r in range(G):
                    lo_half("down", r, j, raw_slot("down"))
                for r in range(G):
                    lo_half("gate", r, j + 1, raw_slot("gate"))
                    lo_half("up", r, j + 1, raw_slot("up"))
            for r in range(G):
                lo_half("down", r, NJ - 1, raw_slot("down"))

        @block.tensor
        def _(pe):
            def three(dst, pairs, **flags):
                for n, ((l_hi, l_lo), (r_hi, r_lo)) in enumerate(pairs):
                    pe.matmul(dst, l_hi, r_hi, start=(n == 0 and flags.get("first", True)), stop=False)
                    pe.matmul(dst, l_hi, r_lo, start=False, stop=False)
                    last = pe.matmul(dst, l_lo, r_hi, start=False, stop=(n == len(pairs) - 1 and flags.get("last", True)))
                return last

            def turn(no, blocks):
                dst_bank = turn_bank[no % TURN_RING]
                if no >= TURN_RING:
                    pe.wait_ge(turn_free, no - TURN_RING + 1)
                for n, src in enumerate(blocks):
                    last = pe.transpose(dst_bank[:, n * P:(n + 1) * P], src, ident[:])
                last.then_inc(turn_full, 1)

            def bank_of_product(no):
                if no >= PROD_RING:
                    pe.wait_ge(prod_free, no - PROD_RING + 1)
                return prod_bank[no % PROD_RING]

            def cols(t_hi, t_lo, k, a, b):
                return t_hi[:, k, a:b], t_lo[:, k, a:b]

            def product(kind, n, k, lhs, a, rhs, b, width=W):
                no = prod_no[kind, n, k]
                three(bank_of_product(no)[:, 0:width], [(cols(*lhs, k, a, a + P), cols(*rhs, k, b, b + width)) for k in range(KT)]
                      ).then_inc(prod_full, 1)

            def turn_probs(n, g):
                turn(turn_no["probs", n, g], [raw[:, n % 2, t * P:(t + 1) * P] for t in key_tiles(n)[g]])

            def attend_group(n, g):
                keys, slot = key_tiles(n)[g], group_no[n, g] % PT_RING
                pe.wait_ge(turn_free, turn_no["probs", n, g] + 1)
                three(o_bank[:], [((pT_hi[:, slot, b * P:(b + 1) * P], pT_lo[:, slot, b * P:(b + 1) * P]),
                                   (v_hi[:, t, :], v_lo[:, t, :])) for b, t in enumerate(keys)],
                      first=(g == 0), last=(g == len(key_tiles(n)) - 1)).then_inc(group_attended, 1)

            pe.wait_ge(consts_ready, 2)
            for kind, n, k in steps:
                if kind == "xn_turn":
                    pe.wait_ge(xn_ready, (n + 1) * TC)
                    turn(turn_no[kind, n, k], [xw[:, t, k * P:(k + 1) * P] for t in range(TC)])
                elif kind == "xh_turn":
                    pe.wait_ge(xh_ready, n + 1)
                    turn(turn_no[kind, n, k], [xh[:, t, k * P:(k + 1) * P] for t in range(TC)])
                elif kind in ("qk_weight", "vo_weight"):
                    left, right = (0, 1) if kind == "qk_weight" else (2, 3)
                    no = prod_no[kind, n, k]
                    dst = bank_of_product(no)
                    for q in range(KT):
                        if k == 0:
                            pe.wait_ge(w_ready[left], q + 1)
                            pe.wait_ge(w_ready[right], q + 1)
                        last = three(dst[:], [(cols(*turned[left], q, k * P, (k + 1) * P), cols(*turned[right], q, 0, W))],
                                     first=(q == 0), last=(q == KT - 1))
                    last.then_inc(prod_full, 1)
                elif kind == "z":
                    pe.wait_ge(prod_free, prod_no["qk_weight", 0, KT - 1] + 1)
                    pe.wait_ge(turn_free, turn_no["xh_turn", n, KT - 1] + 1)
                    product(kind, n, k, (mu_hi, mu_lo), k * P, (xT_hi, xT_lo), n * W)
                elif kind == "v":
                    pe.wait_ge(prod_free, prod_no["vo_weight", 0, KT - 1] + 1)
                    pe.wait_ge(turn_free, turn_no["xh_turn", n, KT - 1] + 1)
                    product(kind, n, k, (xT_hi, xT_lo), n * W + k * P, (vo_hi, vo_lo), 0)
                elif kind == "scores":
                    pe.wait_ge(prod_free, prod_no["z", n // TC, KT - 1] + 1)
                    for g, keys in enumerate(key_tiles(n)):
                        product(kind, n, g, (zg_hi, zg_lo), n % TC * P, (xT_hi, xT_lo), g * W, len(keys) * P)
                elif kind == "head":
                    pe.wait_ge(exp_ready, n + 1)
                    for g in groups_of(kind, n):
                        turn_probs(n, g)
                elif kind == "attend":
                    if n >= 1:
                        pe.wait_ge(rows_ready, n)
                    pe.wait_ge(prod_free, prod_no["v", n // TC, n % TC] + 1)
                    for g in range(len(key_tiles(n))):
                        if g + HEAD < len(key_tiles(n)):
                            turn_probs(n, g + HEAD)
                        attend_group(n, g)

            pe.wait_ge(prod_free, len(prod_no))
            pe.wait_ge(turn_free, len(turn_no))

            def gate_up(j, c):
                for r in range(G):
                    fill = j * (NCH * G) + (c * G + r)
                    if type(j) is not int or c or j or r >= 2:
                        pe.wait_ge(hid_ready, fill - 1)
                    for m, banks, full in (("gate", gate_bank, gate_full), ("up", up_bank, up_full)):
                        if c == 0:
                            pe.wait_ge(wt_lo[m], j * G + (r + 1))
                        wh, wl = weight_hi[m], weight_lo[m]
                        for k in range(KT):
                            lhs_hi, lhs_lo = wh[:, k, r * P:(r + 1) * P], wl[:, k, r * P:(r + 1) * P]
                            rhs_hi, rhs_lo = cols(xT_hi, xT_lo, k, c * W, (c + 1) * W)
                            pe.matmul(banks[r % 2][:], lhs_hi, rhs_hi, start=(k == 0), stop=False)
                            pe.matmul(banks[r % 2][:], lhs_hi, rhs_lo, start=False, stop=False)
                            last = pe.matmul(banks[r % 2][:], lhs_lo, rhs_hi, start=False, stop=(k == KT - 1))
                        last.then_inc(full, 1)

            def down(j, c, peeled_first=False, units=(hs_hi, hs_lo), banks=down_bank):
                if c == 0:
                    pe.wait_ge(wt_lo["down"], j * G + G)
                for t in range(TC):
                    if banks is not down_bank:
                        pe.wait_ge(hid_ready, NJ * NCH * G)
                    elif not peeled_first:
                        pe.wait_ge(added, j * NT + (c * TC + t) - (TC - 1))
                    for r in range(G):
                        if t == 0:
                            pe.wait_ge(hs_ready, j * (NCH * G) + (c * G + r + 1))
                        s_hi, s_lo = (u[:, r, t * P:(t + 1) * P] for u in units)
                        pe.matmul(banks[t][:], s_hi, dw_hi[:, r, :], start=(r == 0), stop=False)
                        pe.matmul(banks[t][:], s_hi, dw_lo[:, r, :], start=False, stop=False)
                        last = pe.matmul(banks[t][:], s_lo, dw_hi[:, r, :], start=False, stop=(r == G - 1))
                    last.then_inc(down_full, 1)

            def block_of_weights(j, last):
                for c in range(1, NCH):
                    if type(j) is int and j == 0:
                        pe.wait_ge(xnT_loaded[c], 32)
                    gate_up(j, c)
                    down(j, c - 1, peeled_first=(type(j) is int and j == 0 and c == 1))
                if not last:
                    gate_up(j + 1, 0)
                if last:
                    down(j, NCH - 1, units=last_units, banks=last_bank)
                else:
                    down(j, NCH - 1)

            pe.wait_ge(xnT_loaded[0], 32)
            gate_up(0, 0)
            pe.wait_ge(rows_ready, NT)
            block_of_weights(0, False)
            with pe.Fori(1, NJ - 1) as j:
                block_of_weights(j, False)
            block_of_weights(NJ - 1, True)

        @block.scalar
        def _(act):
            def exponentials(n):
                act.wait_ge(max_ready, n + 1)
                probs = raw[:, n % 2, 0:(n + 1) * P]
                nc.scalar.activation(probs, probs, ACT.Exp, bias=neg_max[:, n % 2:n % 2 + 1], scale=SCALE,
                                     accum_out=row_sum[:, n:n + 1]).then_inc(exp_ready, 1)

            def probs_hi(n, g):
                no, gno = turn_no["probs", n, g], group_no[n, g]
                act.wait_ge(turn_full, no + 1)
                if gno >= PT_RING:
                    act.wait_ge(group_attended, gno - PT_RING + 1)
                width = len(key_tiles(n)[g]) * P
                nc.scalar.copy(pT_hi[:, gno % PT_RING, 0:width], turn_bank[no % TURN_RING][:, 0:width]).then_inc(turn_hi, 1)

            def hi_half(m, r, slot):
                nc.scalar.copy(piece(m, r, weight_hi[m]), raw_piece(m, r, slot)).then_inc(wt_hi[m], 1)

            affines = 0
            for kind, n, k in steps:
                if kind == "split":
                    act.wait_ge(w_loaded[n][k], 16)
                    nc.scalar.copy(turned[n][0][:, k, :], w_raw(n, k)).then_inc(w_hi_ready[n], 1)
                elif kind == "x_scale":
                    act.wait_ge(rstd2_ready, n + 1)
                    if n:
                        act.wait_ge(turn_full, turn_no["xh_turn", n - 1, KT - 1] + 1)
                    for t in range(TC):
                        act.wait_ge(xn_ready, n * TC + t + 1)
                        last = nc.scalar.activation(xh[:, t, :], xw[:, t, :], ACT.Identity, scale=rstd2[:, t:t + 1])
                    last.then_inc(xh_ready, 1)
                elif kind == "xn_turn":
                    no = turn_no[kind, n, k]
                    act.wait_ge(turn_full, no + 1)
                    if k == KT - 1 and n + 1 < NCH:
                        act.wait_ge(xh_ready, n + 1)
                        act.dma_start(xw[:], x_chunks[n + 1]).then_inc(x_loaded, 16)
                    if (n, k) >= (0, 2):
                        act.wait_ge(xnT_stored[k % 2], 32 * ((n * KT + k) // 2))
                    nc.scalar.copy(stage_hi[:, k % 2, :], turn_bank[no % TURN_RING][:]).then_inc(turn_hi, 1)
                elif kind == "xh_turn":
                    no = turn_no[kind, n, k]
                    b = turn_bank[no % TURN_RING]
                    act.wait_ge(turn_full, no + 1)
                    if (n, k) == (0, 0):
                        act.wait_ge(affine_loaded, 32)
                    affines += 1
                    nc.scalar.activation(b[:], b[:], ACT.Identity, bias=beta_t[:, k:k + 1],
                                         scale=gamma_t[:, k:k + 1]).then_inc(turn_affine, 1)
                    act.wait_ge(turn_affine, affines)
                    nc.scalar.copy(xT_hi[:, k, n * W:(n + 1) * W], b[:]).then_inc(turn_hi, 1)
                elif kind in ("qk_weight", "vo_weight", "z", "v"):
                    no = prod_no[kind, n, k]
                    dst = {"qk_weight": mu_hi, "vo_weight": vo_hi, "z": zg_hi, "v": v_hi[:, n * TC:(n + 1) * TC, :]}[kind]
                    act.wait_ge(prod_full, no + 1)
                    nc.scalar.copy(dst[:, k, :], prod_bank[no % PROD_RING][:]).then_inc(prod_hi, 1)
                elif kind == "head":
                    for g in groups_of(kind, n):
                        probs_hi(n, g)
                elif kind == "attend":
                    for g in groups_of(kind, n):
                        probs_hi(n, g)
                        if g == HEAD and n + 1 < NT:
                            exponentials(n + 1)
                elif kind == "exp":
                    exponentials(n)
                elif kind == "first_split":
                    act.wait_ge(raw_loaded[n], 16)
                    act.wait_ge(prod_full, len(prod_no) if n == "gate" else prod_no["z", NCH - 1, KT - 1] + 1)
                    hi_half(n, k, first_slot(n))

            def chunk(j, c, split_next, split_down, units=hs_hi):
                first = type(j) is int and j == 0 and c == 0
                for r in range(G + 1):
                    fill = j * (NCH * G) + (c * G + r)
                    if r < G:
                        act.wait_ge(gate_full, fill + 1)
                        if not (first and r < 2):
                            act.wait_ge(hid_ready, fill - 1)
                        nc.scalar.activation(rows[:, r % 2, :], gate_bank[r % 2][:], ACT.Silu).then_inc(silu_ready, 1)
                    if split_down and r == 0:
                        act.wait_ge(raw_loaded["down"], j * 16 + 16)
                        if not (type(j) is int and j == 0):
                            act.wait_ge(down_full, j * NT)
                        for q in range(G):
                            hi_half("down", q, raw_slot("down"))
                    if r >= 1:
                        act.wait_ge(hid_ready, fill)
                        if r == 1 and not first:
                            act.wait_ge(pick_step, (j * NCH + c) * PICK - (PICK - 4))
                        nc.scalar.activation(mag[:, r - 1, :], hid[:, r - 1, :], ACT.Abs).then_inc(mag_ready, 1)
                        if split_next:
                            for m, full in (("gate", gate_full), ("up", up_full)):
                                if r == 1:
                                    act.wait_ge(raw_loaded[m], j * 16 + 32)
                                act.wait_ge(full, fill)
                                hi_half(m, r - 1, raw_slot(m))
                if not first and units is hs_hi:
                    act.wait_ge(down_full, (j * NCH + c) * TC)
                for r in range(G):
                    act.wait_ge(picked, j * (NCH * G) + (c * G + r + 1))
                    nc.scalar.copy(units[:, r, :], hid[:, r, :]).then_inc(hs_hi_ready, 1)

            def block_of_weights(j, last):
                for c in range(1, NCH):
                    chunk(j, c, split_next=(c == NCH - 1 and not last), split_down=(c == 1),
                          units=last_units[0] if last and c == NCH - 1 else hs_hi)
                if not last:
                    chunk(j + 1, 0, False, False)

            act.wait_ge(resid_stored, 16 * NT)
            chunk(0, 0, False, False)
            block_of_weights(0, False)
            with act.Fori(1, NJ - 1) as j:
                block_of_weights(j, False)
            block_of_weights(NJ - 1, True)

        @block.vector
        def _(dve):
            made = [0]

            def step(ins):
                made[0] += 1
                ins.then_inc(vec_step, 1)
                return made[0]

            def lo_of_turned(no, dst_lo, src_hi):
                dve.wait_ge(turn_hi, no + 1)
                width = src_hi.shape[-1]
                nc.vector.tensor_tensor(dst_lo, turn_bank[no % TURN_RING][:, 0:width], src_hi.bitcast(F32),
                                        ALU.subtract).then_inc(turn_free, 1)

            def probs_lo(n, g):
                width, slot = len(key_tiles(n)[g]) * P, group_no[n, g] % PT_RING
                lo_of_turned(turn_no["probs", n, g], pT_lo[:, slot, 0:width], pT_hi[:, slot, 0:width])

            for kind, n, k in steps:
                if kind == "split":
                    dve.wait_ge(w_hi_ready[n], k + 1)
                    nc.vector.tensor_tensor(turned[n][1][:, k, :], w_raw(n, k), turned[n][0][:, k, :].bitcast(F32),
                                            ALU.subtract).then_inc(w_ready[n], 1)
                elif kind == "x_stats":
                    dve.wait_ge(x_loaded, 16 * (n + 1))
                    for t in range(TC):
                        done = step(nc.vector.bn_stats(stats[:, t, :], xw[:, t, :]))
                    dve.wait_ge(vec_step, done)
                    for t in range(TC):
                        last = nc.vector.bn_aggr(mean_var[:, t, :], stats[:, t, :])
                    last.then_inc(stats_ready, 1)
                elif kind == "x_scale":
                    dve.wait_ge(stats_ready, n + 1)
                    dve.wait_ge(rstd_ready, n + 1)
                    own = slice(n * TC, (n + 1) * TC)
                    nc.vector.tensor_scalar(one_rstd[:, own], rstd[:], 1.0, None, ALU.add)
                    nc.vector.scalar_tensor_tensor(out=neg_mean_rstd[:, own], in0=mean_var[:, :, 0], scalar=-1.0, in1=rstd[:],
                                                   op0=ALU.mult, op1=ALU.mult)
                    for t in range(TC):
                        nc.vector.tensor_scalar(xw[:, t, :], xw[:, t, :], mean_var[:, t, 0:1], rstd[:, t:t + 1],
                                                ALU.subtract, ALU.mult).then_inc(xn_ready, 1)
                elif kind == "xn_turn":
                    if (n, k) >= (0, 2):
                        dve.wait_ge(xnT_stored[k % 2], 32 * ((n * KT + k) // 2))
                    lo_of_turned(turn_no[kind, n, k], stage_lo[:, k % 2, :], stage_hi[:, k % 2, :])
                elif kind == "xh_turn":
                    own = slice(n * W, (n + 1) * W)
                    lo_of_turned(turn_no[kind, n, k], xT_lo[:, k, own], xT_hi[:, k, own])
                elif kind in ("qk_weight", "vo_weight", "z", "v"):
                    if (kind, n, k) == ("v", NCH - 1, 0):
                        for stored in xnT_stored:
                            dve.wait_ge(stored, 16 * KT * NCH)
                    no = prod_no[kind, n, k]
                    dst_hi, dst_lo = {"qk_weight": (mu_hi, mu_lo), "vo_weight": (vo_hi, vo_lo), "z": (zg_hi, zg_lo),
                                      "v": (v_hi[:, n * TC:(n + 1) * TC, :], v_lo[:, n * TC:(n + 1) * TC, :])}[kind]
                    dve.wait_ge(prod_hi, split_no[kind, n, k] + 1)
                    nc.vector.tensor_tensor(dst_lo[:, k, :], prod_bank[no % PROD_RING][:], dst_hi[:, k, :].bitcast(F32),
                                            ALU.subtract).then_inc(prod_free, 1)
                elif kind == "scores":
                    groups, slot, parts = key_tiles(n), n % 2, 0
                    if n >= 2:
                        dve.wait_ge(exp_ready, n - 1)
                    for g, keys in enumerate(groups):
                        no = prod_no[kind, n, g]
                        src = prod_bank[no % PROD_RING]
                        dve.wait_ge(prod_full, no + 1)
                        full = len(keys) * P - (P if g == len(groups) - 1 else 0)
                        if full:
                            last = nc.vector.tensor_scalar(raw[:, slot, g * W:g * W + full], src[:, 0:full], 1.0, None, ALU.mult,
                                                           ALU.max, accum_out=part_max[:, slot, parts:parts + 1])
                            parts += 1
                            if g < len(groups) - 1:
                                last.then_inc(prod_free, 1)
                    diagonal = raw[:, slot, n * P:(n + 1) * P]
                    nc.vector.tensor_tensor(diagonal, src[:, full:full + P], causal[:], ALU.add).then_inc(prod_free, 1)
                    dve.wait_ge(prod_free, prod_no[kind, n, len(groups) - 1] + 1)
                    done = step(nc.vector.reduce_max(part_max[:, slot, parts:parts + 1], diagonal, AX.X))
                    dve.wait_ge(vec_step, done)
                    done = step(nc.vector.reduce_max(row_max[:, slot:slot + 1], part_max[:, slot, 0:parts + 1], AX.X))
                    dve.wait_ge(vec_step, done)
                    nc.vector.tensor_scalar(neg_max[:, slot:slot + 1], row_max[:, slot:slot + 1], -SCALE, None,
                                            ALU.mult).then_inc(max_ready, 1)
                elif kind == "head":
                    for g in groups_of(kind, n):
                        probs_lo(n, g)
                    slot = n % 2
                    dve.wait_ge(rows_loaded[slot], 16 * (n // 2 + 1))
                    step(nc.vector.tensor_scalar(rows[:, slot, :], rows[:, slot, :], one_rstd[:, n:n + 1],
                                                 neg_mean_rstd[:, n:n + 1], ALU.mult, ALU.add))
                    inverse_made = step(nc.vector.reciprocal(inv_sum[:, n:n + 1], row_sum[:, n:n + 1]))
                elif kind == "attend":
                    slot = n % 2
                    for g in groups_of(kind, n):
                        probs_lo(n, g)
                    dve.wait_ge(vec_step, inverse_made)
                    dve.wait_ge(group_attended, group_no[n, len(key_tiles(n)) - 1] + 1)
                    nc.vector.scalar_tensor_tensor(out=rows[:, slot, :], in0=o_bank[:], scalar=inv_sum[:, n:n + 1],
                                                   in1=rows[:, slot, :], op0=ALU.mult, op1=ALU.add).then_inc(rows_ready, 1)

            def add_down(j, c, banks=down_bank):
                for t in range(TC):
                    tile = c * TC + t
                    dve.wait_ge(down_full, j * NT + (tile + 1))
                    nc.vector.tensor_tensor(acc[:, tile, :], banks[t][:], acc[:, tile, :], ALU.add).then_inc(added, 1)

            def chunk(j, c, before, units=(hs_hi, hs_lo)):
                base = j * (NCH * G) + c * G
                if before is not None:
                    dve.wait_ge(hs_ready, base)
                for r in range(G):
                    dve.wait_ge(silu_ready, base + (r + 1))
                    dve.wait_ge(up_full, base + (r + 1))
                    nc.vector.tensor_tensor(hid[:, r, :], rows[:, r % 2, :], up_bank[r % 2][:], ALU.mult).then_inc(hid_ready, 1)
                dve.wait_ge(mag_ready, base + G)
                picks = (j * NCH + c) * PICK
                nc.vector.tensor_tensor(beats_a[:], mag[:, 0:G:2, :], mag[:, 1:G:2, :], ALU.is_ge).then_inc(pick_step, 1)
                nc.vector.tensor_tensor(beats_b[:], mag[:, 0:2, :], mag[:, 2:4, :], ALU.is_ge).then_inc(pick_step, 1)
                nc.vector.tensor_tensor(beats_c[:, 0, :], mag[:, 0, :], mag[:, 3, :], ALU.is_ge).then_inc(pick_step, 1)
                nc.vector.tensor_tensor(beats_c[:, 1, :], mag[:, 1, :], mag[:, 2, :], ALU.is_ge).then_inc(pick_step, 1)
                dve.wait_ge(pick_step, picks + 4)
                nc.vector.tensor_tensor(pair_sum[:], beats_b[:], beats_c[:], ALU.add).then_inc(pick_step, 1)
                dve.wait_ge(pick_step, picks + 5)
                nc.vector.tensor_tensor(beats_b[:, 0, :], beats_b[:, 0, :], beats_c[:, 1, :], ALU.add).then_inc(pick_step, 1)
                nc.vector.tensor_tensor(beats_b[:, 1, :], beats_b[:, 1, :], beats_c[:, 0, :], ALU.add).then_inc(pick_step, 1)
                dve.wait_ge(pick_step, picks + 7)
                nc.vector.tensor_tensor(pair_sum[:, 0, :], pair_sum[:, 0, :], beats_a[:, 0, :], ALU.add).then_inc(pick_step, 1)
                nc.vector.tensor_tensor(pair_sum[:, 1, :], pair_sum[:, 1, :], beats_a[:, 0, :], ALU.subtract).then_inc(pick_step, 1)
                nc.vector.tensor_tensor(beats_b[:, 0, :], beats_a[:, 1, :], beats_b[:, 0, :], ALU.subtract).then_inc(pick_step, 1)
                nc.vector.tensor_tensor(beats_b[:, 1, :], beats_b[:, 1, :], beats_a[:, 1, :], ALU.add).then_inc(pick_step, 1)
                dve.wait_ge(pick_step, picks + PICK)
                rules = ((pair_sum[:, 0, :], 2.0, ALU.is_ge), (pair_sum[:, 1, :], 1.0, ALU.is_ge),
                         (beats_b[:, 0, :], 0.0, ALU.is_ge), (beats_b[:, 1, :], 1.0, ALU.is_le))
                u_hi, u_lo = units

                def keep(r):
                    wins, bound, rule = rules[r]
                    nc.vector.scalar_tensor_tensor(out=hid[:, r, :], in0=wins, scalar=bound, in1=hid[:, r, :], op0=rule,
                                                   op1=ALU.mult).then_inc(picked, 1)

                def lo_of_units(r):
                    dve.wait_ge(hs_hi_ready, base + (r + 1))
                    nc.vector.tensor_tensor(u_lo[:, r, :], hid[:, r, :], u_hi[:, r, :].bitcast(F32), ALU.subtract).then_inc(hs_ready, 1)

                if u_hi is hs_hi:
                    for r in range(G):
                        keep(r)
                    if before is not None:
                        add_down(*before)
                    for r in range(G):
                        lo_of_units(r)
                else:
                    keep(0)
                    for r in range(1, G):
                        keep(r)
                        lo_of_units(r - 1)
                    lo_of_units(G - 1)
                    add_down(*before)

            def block_of_weights(j, last):
                for c in range(1, NCH):
                    chunk(j, c, (j, c - 1), units=last_units if last and c == NCH - 1 else (hs_hi, hs_lo))
                if not last:
                    chunk(j + 1, 0, (j, NCH - 1))
                else:
                    add_down(j, NCH - 1, last_bank)

            chunk(0, 0, None)
            dve.wait_ge(acc_loaded, 16 * NCH)
            block_of_weights(0, False)
            with dve.Fori(1, NJ - 1) as j:
                block_of_weights(j, False)
            block_of_weights(NJ - 1, True)


INPUTS = ["L0_attn_x", "L0_attn_qkv", "L0_attn_o_proj", "L0_attn_gamma", "L0_attn_beta",
          "L0_ffn_w_gate", "L0_ffn_w_up", "L0_ffn_w_down"]


def kernel(**inputs):
    import numpy as np
    import concourse.bacc as bacc
    from concourse.bass_utils import run_bass_kernel_spmd

    nc = bacc.Bacc("TRN2", target_bir_lowering=False, num_devices=1)
    arrays, args = {}, []
    for name in INPUTS:
        a = np.asarray(inputs[name])
        if a.ndim == 1:
            a = a.reshape(-1, P).T
        if name == "L0_attn_qkv":
            a = a.T
        a = np.ascontiguousarray(a)
        arrays[name] = a
        args.append(nc.dram_tensor(name, a.shape, mybir.dt.from_np(a.dtype), kind="ExternalInput").ap())
    shape = arrays["L0_attn_x"].shape
    result = nc.dram_tensor("result", shape, F32, kind="ExternalOutput").ap()
    attention_ffn(nc, *args, result)
    r = run_bass_kernel_spmd(nc, [arrays], core_ids=[0])
    return r.results[0]["result"]
```
